# Optimizing a Trainium2 kernel written in Bass

```python
import numpy as np
import jax
import jax.numpy as jnp

def _softmax(x, axis=-1):
    return jax.nn.softmax(x, axis=axis)

def _gelu(x):
    return jax.nn.gelu(x, approximate=True)

def _silu(x):
    return jax.nn.silu(x)

def _sigmoid(x):
    return jax.nn.sigmoid(x)

def _layernorm(x, axis=-1, eps=1e-05):
    m = jnp.mean(x, axis=axis, keepdims=True)
    v = jnp.var(x, axis=axis, keepdims=True)
    return (x - m) / jnp.sqrt(v + eps)

def _scatter_add(tgt, idx, src, axis=0):
    return tgt.at[idx].add(src)

def _segment_sum(src, seg, n):
    return jax.ops.segment_sum(src, seg, n)
kernel_name = 'mk_sandwich_d1_jaxref_r8_b83e02'

def setup_inputs(seed: int=0):
    np.random.seed(seed)
    _w = jnp.asarray

    def _L0_attn_setup():
        import jax, jax.numpy as jnp
        import numpy as np
        DIM = 128
        HEADS = 1
        HDIM = DIM // HEADS
        INNER = 16
        B, L = (2, 512)
        ROPE_BASE = 32.0

        def _apply_rope(x, pos, base):
            d = x.shape[-1]
            inv_freq = base ** (-jnp.arange(0, d, 2, dtype=jnp.float32) / d)
            ang = pos[:, None].astype(jnp.float32) * inv_freq
            emb = jnp.concatenate([ang, ang], axis=-1)
            cos = jnp.cos(emb)[None, :, None, :].astype(x.dtype)
            sin = jnp.sin(emb)[None, :, None, :].astype(x.dtype)
            x1, x2 = (x[..., :d // 2], x[..., d // 2:])
            rot = jnp.concatenate([-x2, x1], axis=-1)
            return x * cos + rot * sin
        key = jax.random.key(seed)
        ks = jax.random.split(key, 7)
        hidden_states = jax.random.normal(ks[0], (B, L, DIM), dtype=jnp.float32)
        Wq = jax.random.normal(ks[1], (DIM, DIM), dtype=jnp.float32) * 0.02
        Wk = jax.random.normal(ks[2], (DIM, DIM), dtype=jnp.float32) * 0.02
        fc1_w = jax.random.normal(ks[3], (INNER, 1), dtype=jnp.float32) * 0.1
        fc1_b = jax.random.normal(ks[4], (INNER,), dtype=jnp.float32) * 0.1
        fc2_w = jax.random.normal(ks[5], (DIM, INNER), dtype=jnp.float32) * 0.1
        fc2_b = jax.random.normal(ks[6], (DIM,), dtype=jnp.float32) * 0.1
        return {'hidden_states': hidden_states, 'Wq': Wq, 'Wk': Wk, 'fc1_w': fc1_w, 'fc1_b': fc1_b, 'fc2_w': fc2_w, 'fc2_b': fc2_b}
    _L0_attn_in = _L0_attn_setup()

    def _L0_ffn_setup():
        import jax, jax.numpy as jnp
        import numpy as np
        B, S, D, O, H, E, K = (4, 128, 128, 128, 256, 16, 4)
        key = jax.random.key(seed)
        ks = jax.random.split(key, 8)
        x = jax.random.normal(ks[0], (B, S, D), dtype=jnp.float32)
        w_gate = jax.random.normal(ks[1], (D, E), dtype=jnp.float32) * 0.01
        w_noise = jnp.zeros((D, E), dtype=jnp.float32)
        W1 = jax.random.normal(ks[2], (E, D, H), dtype=jnp.float32) * (1.0 / np.sqrt(D))
        b1 = jnp.zeros((E, H), dtype=jnp.float32)
        W2 = jax.random.normal(ks[3], (E, H, O), dtype=jnp.float32) * (1.0 / np.sqrt(H))
        b2 = jnp.zeros((E, O), dtype=jnp.float32)
        return {'x': x, 'w_gate': w_gate, 'w_noise': w_noise, 'W1': W1, 'b1': b1, 'W2': W2, 'b2': b2}
    _L0_ffn_in = _L0_ffn_setup()
    _d = {'L0_attn_hidden_states': _L0_attn_in['hidden_states'], 'L0_attn_Wq': _L0_attn_in['Wq'], 'L0_attn_Wk': _L0_attn_in['Wk'], 'L0_attn_fc1_w': _L0_attn_in['fc1_w'], 'L0_attn_fc1_b': _L0_attn_in['fc1_b'], 'L0_attn_fc2_w': _L0_attn_in['fc2_w'], 'L0_attn_fc2_b': _L0_attn_in['fc2_b'], 'L0_ffn_w_gate': _L0_ffn_in['w_gate'], 'L0_ffn_w_noise': _L0_ffn_in['w_noise'], 'L0_ffn_W1': _L0_ffn_in['W1'], 'L0_ffn_b1': _L0_ffn_in['b1'], 'L0_ffn_W2': _L0_ffn_in['W2'], 'L0_ffn_b2': _L0_ffn_in['b2']}
    _x0 = _d['L0_attn_hidden_states']
    _d['L0_attn_hidden_states'] = jax.random.normal(jax.random.fold_in(jax.random.key(seed), 1), (2, 2048, 128), dtype=_x0.dtype)
    del _x0
    return _d

def reference(L0_attn_hidden_states, L0_attn_Wq, L0_attn_Wk, L0_attn_fc1_w, L0_attn_fc1_b, L0_attn_fc2_w, L0_attn_fc2_b, L0_ffn_w_gate, L0_ffn_w_noise, L0_ffn_W1, L0_ffn_b1, L0_ffn_W2, L0_ffn_b2):

    def _L0_attn_ref(hidden_states, Wq, Wk, fc1_w, fc1_b, fc2_w, fc2_b):
        import jax, jax.numpy as jnp
        import numpy as np
        DIM = 128
        HEADS = 1
        HDIM = DIM // HEADS
        INNER = 16
        B, L = (2, 512)
        ROPE_BASE = 32.0

        def _apply_rope(x, pos, base):
            d = x.shape[-1]
            inv_freq = base ** (-jnp.arange(0, d, 2, dtype=jnp.float32) / d)
            ang = pos[:, None].astype(jnp.float32) * inv_freq
            emb = jnp.concatenate([ang, ang], axis=-1)
            cos = jnp.cos(emb)[None, :, None, :].astype(x.dtype)
            sin = jnp.sin(emb)[None, :, None, :].astype(x.dtype)
            x1, x2 = (x[..., :d // 2], x[..., d // 2:])
            rot = jnp.concatenate([-x2, x1], axis=-1)
            return x * cos + rot * sin
        b, l, _ = hidden_states.shape
        q = (hidden_states @ Wq.T).reshape(b, l, HEADS, HDIM).astype(jnp.bfloat16)
        k = (hidden_states @ Wk.T).reshape(b, l, HEADS, HDIM).astype(jnp.bfloat16)
        pos = jnp.arange(l)
        q = _apply_rope(q, pos, ROPE_BASE)
        k = _apply_rope(k, pos, ROPE_BASE)
        scores = jnp.einsum('bqhd,bkhd->bhqk', q.astype(jnp.float32), k.astype(jnp.float32)) / HDIM ** 0.5
        causal = jnp.tril(jnp.ones((l, l), dtype=bool))
        exp_qk = jnp.where(causal[None, None], jnp.exp(scores), 0.0)
        o = jnp.swapaxes(exp_qk.sum(axis=-1), 1, 2)
        o = jax.nn.relu(o @ fc1_w.T + fc1_b)
        return o @ fc2_w.T + fc2_b

    def _L0_ffn_ref(x, w_gate, w_noise, W1, b1, W2, b2):
        import jax, jax.numpy as jnp
        import numpy as np
        B, S, D, O, H, E, K = (4, 128, 128, 128, 256, 16, 4)
        logits = jnp.zeros((x.shape[0], x.shape[1], E), dtype=x.dtype).at[..., 1].set(100.0)
        top_vals, top_idx = jax.lax.top_k(logits, K)
        gates_k = jax.nn.softmax(top_vals, axis=-1)
        gates = jnp.einsum('bske,bsk->bse', jax.nn.one_hot(top_idx, E, dtype=x.dtype), gates_k)
        h = jax.nn.relu(jnp.einsum('bsd,edh->ebsh', x, W1) + b1[:, None, None, :])
        y = jnp.einsum('ebsh,eho->ebso', h, W2) + b2[:, None, None, :]
        out = jnp.einsum('ebso,bse->bso', y, gates)
        return out
    x = L0_attn_hidden_states
    x = x + _layernorm(_L0_attn_ref(_layernorm(x, axis=-1), L0_attn_Wq, L0_attn_Wk, L0_attn_fc1_w, L0_attn_fc1_b, L0_attn_fc2_w, L0_attn_fc2_b), axis=-1)
    x = x + _layernorm(_L0_ffn_ref(_layernorm(x, axis=-1), L0_ffn_w_gate, L0_ffn_w_noise, L0_ffn_W1, L0_ffn_b1, L0_ffn_W2, L0_ffn_b2), axis=-1)
    return x

_drawn_inputs = setup_inputs


def setup_inputs(seed=0):
    import zlib

    import numpy as np

    out = dict(_drawn_inputs(seed))
    spreads = {'L0_ffn_w_noise': (0.0, 0.1), 'L0_ffn_b1': (0.0, 0.1), 'L0_ffn_b2': (0.0, 0.1)}
    factors = {}
    for name, (base, spread) in spreads.items():
        noise = np.random.default_rng([zlib.crc32(name.encode()), seed]).standard_normal(out[name].shape)
        drawn = base * np.exp(spread * noise) if base else spread * noise
        out[name] = jnp.asarray(drawn.astype(out[name].dtype))
    for name, factor in factors.items():
        out[name] = (out[name] * factor).astype(out[name].dtype)
    return out
```

```python
import concourse.bass as bass
from concourse import mybir
from contextlib import ExitStack

F32 = mybir.dt.float32
BF16 = mybir.dt.bfloat16
ALU = mybir.AluOpType
ACT = mybir.ActivationFunctionType
AX = mybir.AxisListType

P = 128
TILES = 4
GROUP = TILES * P
HALF = P // 2
INNER = 16
BLOCK = 32
HIDDEN = 256
HC = HIDDEN // P
EXPERT = 1
EPS = 1e-5
MASKED = -1e30
SEGMENT = 1024
PER_SEG = SEGMENT // GROUP


class Signal:

    def __init__(self, ctx, nc, name, owner):
        self.owner = owner
        self.sems = {}
        self.make = lambda who: ctx.enter_context(nc.semaphore(f"{name}_{who}"))

    def sem(self, who):
        if who not in self.sems:
            self.sems[who] = self.make(who)
        return self.sems[who]

    def done(self, instruction, n):
        instruction.then_inc(self.sem(self.owner(n)), 1)

    def wait(self, engine, n):
        who = self.owner(n)
        engine.wait_ge(self.sem(who), sum(self.owner(m) == who for m in range(n + 1)))


class Chain:

    def __init__(self, engine, sem):
        self.engine, self.sem, self.n = engine, sem, 0

    def mark(self, instruction):
        self.n += 1
        instruction.then_inc(self.sem, 1)

    def link(self, instruction):
        self.mark(instruction)
        self.engine.wait_ge(self.sem, self.n)


def segments(gb):
    return -(-(gb + 1) // PER_SEG)


def plan(n_groups, per_batch):
    first = list(range(per_batch))
    mid = first + [g for g in range(n_groups - 1, per_batch - 1, -1)]
    steps = []

    def at(t, name, *args):
        steps.append((t, len(steps), (name, *args)))

    def front(n, t, w):
        for k, name in enumerate(["stat1", "rs1", "norm1", "tr1", "q", "k", "rope"]):
            at(t + w * FRONT_AT[k], name, n)

    for n, (t, w) in enumerate(FRONT_TIMES):
        front(n, t, w)
    for m, g in enumerate(mid):
        gb = g % per_batch
        parts = [(j, s) for j in range(TILES) for s in range(segments(gb))]
        for i, (j, s) in enumerate(parts):
            at(m + i / len(parts), "scores", m, g, j, s)
        for name, d in BACK_AT.items():
            last = m == n_groups - 1
            at(m + (1 + (d - 1) * (0.5 if last else 1)), name, m, g)
    steps.sort()
    return mid, [s for _, _, s in steps]


FRONT_AT = [0, 0.1, 0.2, 0.35, 0.5, 0.6, 0.85]
FRONT_TIMES = [(-1, 0.9), (-0.6, 0.9), (0.0, 0.9), (0.5, 0.9), (1.0, 0.9), (1.5, 0.9), (2.0, 0.9), (2.5, 0.9)]
BACK_AT = {"fc1": 1.08, "hT": 1.12, "fc2": 1.2, "stat3": 1.26, "rs3": 1.32, "x1": 1.42, "stat4": 1.46,
           "rs4": 1.5, "norm4": 1.56, "trz": 1.7, "h0": 1.8, "h1": 1.88, "y": 2.1, "stat5": 2.2, "rs5": 2.26,
           "out": 2.4}


def owners(mid, per_batch):
    heavy = [m for m, g in enumerate(mid) if g % per_batch >= 2]
    return {
        "tr1": lambda n: "act",
        "q": lambda n: "act", "k": lambda n: "act",
        "hT": lambda n: "act",
        "stat3": lambda n: "dve" if n in heavy else "act",
        "trz": lambda n: "act",
        "h0": lambda n: "act", "h1": lambda n: "dve",
        "stat5": lambda n: "act",
    }


def build(nc, x, tables, wq_t, wk_t, fc1_w, fc1_b, fc2_wt, fc2_b, w1, b1, w2, b2, out):
    batch, length, dim = x.shape
    n_groups = batch * length // GROUP
    per_batch = length // GROUP
    mid, ORDER = plan(n_groups, per_batch)
    own = owners(mid, per_batch)
    SCALE = 1.0 / float(dim) ** 0.5

    x_v = x.rearrange("b (g j p) d -> (b g) p j d", j=TILES, p=P)
    out_v = out.rearrange("b (g j p) d -> (b g) p j d", j=TILES, p=P)

    with ExitStack() as ctx:
        def sb(name, shape, dt):
            return ctx.enter_context(nc.sbuf_tensor(name, shape, dt))

        def sem(name):
            return ctx.enter_context(nc.semaphore(name))

        def signal(name, owner):
            return Signal(ctx, nc, name, owner if callable(owner) else lambda n: owner)

        ident = sb("ident", [P, P], F32)
        ident_b = sb("ident_b", [P, P], BF16)
        later = sb("later", [P, P], BF16)
        ones_b = sb("ones_b", [P, P], BF16)
        half_neg = sb("half_neg", [P, TILES], F32)
        table = sb("table", [P, 2, length], BF16)
        wqk = sb("wqk", [P, 2, P], F32)
        fc1 = sb("fc1", [P, 2, INNER], F32)
        fc2 = sb("fc2", [P, TILES, P], F32)
        w1_s = sb("w1_s", [P, HIDDEN], F32)
        b1_s = sb("b1_s", [P, HC], F32)
        w2_s = sb("w2_s", [P, HC, P], F32)
        b2_f = sb("b2_f", [P, P], F32)
        b2_r = sb("b2_r", [P, 2, P], F32)
        b2_h = sb("b2_h", [P, 3, P], BF16)
        b2_s = sb("b2_s", [P, TILES, P], BF16)
        means = sb("means", [P, 4], F32)
        x_s = sb("x_s", [P, n_groups, TILES, P], F32)
        xn = sb("xn", [P, 2, TILES, P], F32)
        xT = sb("xT", [P, 2, GROUP], F32)
        qk = sb("qk", [P, n_groups, 2, GROUP], BF16)
        qk_swap = sb("qk_swap", [P, n_groups, 2, GROUP], BF16)
        rot = sb("rot", [P, 2, 2, 2, GROUP], BF16)
        qk_r = sb("qk_r", [P, n_groups, 2, GROUP], BF16)
        rows = sb("rows", [P, n_groups, 2, TILES], F32)
        osum = sb("osum", [P, n_groups, TILES], F32)
        h1e = sb("h1e", [P, 2, TILES, BLOCK], F32)
        h1T = sb("h1T", [P, 2, P], F32)
        x1 = sb("x1", [P, n_groups, TILES, P], F32)
        z = sb("z", [P, 2, TILES, P], F32)
        zT = sb("zT", [P, 2, GROUP], F32)
        hid = sb("hid", [P, 2, HC, GROUP], F32)
        out_s = sb("out_s", [P, n_groups, TILES, P], F32)
        junk = sb("junk", [P, 2, TILES, P], BF16)
        stats = sb("stats", [P, n_groups, 4, TILES, 6], F32)
        mv = sb("mv", [P, n_groups, 4, TILES, 2], F32)
        neg_mean = sb("neg_mean", [P, n_groups, 2, TILES], F32)
        ve = sb("ve", [P, n_groups, 4, TILES], F32)
        rstd = sb("rstd", [P, n_groups, 4, TILES], F32)
        score = [ctx.enter_context(nc.psum_tensor(f"score{i}", [P, SEGMENT], F32)) for i in range(2)]
        ring = [ctx.enter_context(nc.psum_tensor(f"ring{i}", [P, GROUP], F32)) for i in range(2)]
        net = [ctx.enter_context(nc.psum_tensor(f"net{i}", [P, TILES, P], F32)) for i in range(2)]

        s_x = [sem(f"s_x{g}") for g in range(n_groups)]
        s_table = [sem(f"s_table{c}") for c in range(per_batch)]
        s_swap = [sem(f"s_swap{g}") for g in range(n_groups)]
        s_wqk, s_fc1, s_fc2, s_w1, s_w2, s_b2 = (sem("s_" + n) for n in ["wqk", "fc1", "fc2", "w1", "w2", "b2"])
        s_out = sem("s_out")
        s_zeroed, s_const, s_fc2c, s_b2c = (sem("s_" + n) for n in ["zeroed", "const", "fc2c", "b2c"])
        s_dve, s_pool = sem("s_dve"), sem("s_pool")

        made = {n: signal("made_" + n, "pe") for n in ["tr1", "q", "k", "scores", "hT", "fc2", "trz", "h0", "h1", "y"]}
        taken = {n: signal("taken_" + n, own[n]) for n in ["tr1", "q", "k", "hT", "trz", "h0", "h1"]}
        var = {1: signal("var1", "dve"), 3: signal("var3", own["stat3"]),
               4: signal("var4", "dve"), 5: signal("var5", own["stat5"])}
        ready_r = {n: signal(f"rstd{n}", "pool") for n in [1, 3, 4, 5]}
        normed = {1: signal("normed1", "pool"), 4: signal("normed4", "pool")}
        s_rope = signal("roped", "dve")
        s_exp = signal("exps", "act")
        s_fc1d = signal("fc1d", "dve")
        s_x1 = signal("x1d", "dve")
        s_fin = signal("fin", "dve")

        slot = {1: 0, 3: 1, 4: 2, 5: 3}

        ring_users = [(st[0], st[1]) for st in ORDER if st[0] in taken]
        net_users = [(st[0], st[1]) for st in ORDER if st[0] in ("fc2", "y")]
        segs = [st[1:] for st in ORDER if st[0] == "scores"]
        seg_no = {st: i for i, st in enumerate(segs)}
        last_seg = {m: max(i for i, st in enumerate(segs) if st[0] == m) for m in range(n_groups)}

        def ring_of(name, n):
            return ring[ring_users.index((name, n)) % 2]

        def net_of(name, n):
            return net[net_users.index((name, n)) % 2]

        block = ctx.enter_context(nc.Block())

        def load_x(eng, g):
            eng.dma_start(x_s[:, g], x_v[g]).then_inc(s_x[g], 16)

        def load_table(eng, c):
            eng.dma_start(table[:, :, c * GROUP:(c + 1) * GROUP],
                          tables[:, :, c * GROUP:(c + 1) * GROUP]).then_inc(s_table[c], 16)

        @block.sync
        def _(eng):
            load_x(eng, 0)
            eng.dma_start(wqk[:, 0, :], wq_t).then_inc(s_wqk, 16)
            eng.dma_start(wqk[:, 1, :], wk_t).then_inc(s_wqk, 16)
            load_x(eng, 1)
            load_table(eng, 0)
            load_x(eng, 2)
            load_table(eng, 1)
            load_x(eng, 3)
            eng.wait_ge(s_zeroed, 2)
            for j in range(TILES):
                eng.dma_start(fc2[BLOCK * j:BLOCK * j + INNER, j, :], fc2_wt).then_inc(s_fc2, 16)
                eng.dma_start(fc2[BLOCK * j + INNER:BLOCK * j + INNER + 1, j, :], fc2_b).then_inc(s_fc2, 16)
            for c, v in enumerate([fc1_w, fc1_b]):
                eng.dma_start(fc1[:, c, :], v.partition_broadcast(P)).then_inc(s_fc1, 16)
            eng.dma_start(w2_s[:, :, :], w2[EXPERT].rearrange("(c p) o -> p c o", p=P)).then_inc(s_w2, 16)
            for part in range(3):
                eng.dma_start(b2_f[32 * part:32 * part + 1, :], b2[EXPERT:EXPERT + 1, :]).then_inc(s_b2, 16)
            eng.dma_start(w1_s[:, :], w1[EXPERT]).then_inc(s_w1, 16)
            eng.dma_start(b1_s[:, :], b1[EXPERT]).then_inc(s_w1, 16)
            load_table(eng, 2)
            load_x(eng, 4)
            load_table(eng, 3)
            for g in range(5, n_groups):
                load_x(eng, g)
            for name, n, *rest in ORDER:
                if name == "rope":
                    taken["q"].wait(eng, n)
                    taken["k"].wait(eng, n)
                    eng.dma_start(qk_swap[0:HALF, n], qk[HALF:P, n]).then_inc(s_swap[n], 16)
                    eng.dma_start(qk_swap[HALF:P, n], qk[0:HALF, n]).then_inc(s_swap[n], 16)
                if name == "out":
                    s_fin.wait(eng, n)
                    eng.dma_start(out_v[rest[0]], out_s[:, rest[0]]).then_inc(s_out, 16)
            eng.wait_ge(s_out, 16 * n_groups)

        @block.gpsimd
        def _(eng):
            own_chain = Chain(eng, s_pool)
            eng.memset(half_neg[:, :], -0.5)
            eng.memset(ident[:, :], 0.0)
            eng.memset(ident_b[:, :], 0.0)
            own_chain.link(eng.memset(later[:, :], 0.0))
            eng.affine_select(out=ident[:, :], in_=ident[:, :], compare_op=ALU.not_equal, fill=1.0, base=0,
                              pattern=[[-1, P]], channel_multiplier=1)
            eng.affine_select(out=ident_b[:, :], in_=ident_b[:, :], compare_op=ALU.not_equal, fill=1.0, base=0,
                              pattern=[[-1, P]], channel_multiplier=1)
            own_chain.link(eng.affine_select(out=later[:, :], in_=later[:, :], compare_op=ALU.is_ge, fill=MASKED,
                                             base=0, pattern=[[-1, P]], channel_multiplier=1))
            eng.memset(half_neg[:, 0:1], -0.5).then_inc(s_const, 1)

            def rs(k, m, g):
                var[k].wait(eng, m)
                own_chain.link(eng.tensor_scalar(ve[:, g, slot[k], :], mv[:, g, slot[k], :, 1], EPS, None, ALU.add))
                ready_r[k].done(eng.tensor_tensor(rstd[:, g, slot[k], :], ve[:, g, slot[k], :], half_neg[:, :],
                                                  ALU.pow), m)

            def norm(k, m, g, src, dst, reader):
                if m >= 2:
                    made[reader].wait(eng, m - 2)
                ready_r[k].wait(eng, m)
                for j in range(TILES):
                    last = eng.tensor_scalar(dst[:, m % 2, j, :], src[:, g, j, :], neg_mean[:, g, k // 4, j:j + 1],
                                             rstd[:, g, slot[k], j:j + 1], ALU.add, ALU.mult)
                normed[k].done(last, m)

            for name, m, *rest in ORDER:
                if name == "rs1":
                    rs(1, m, m)
                elif name in ("rs3", "rs4", "rs5"):
                    rs(int(name[2]), m, rest[0])
                elif name == "norm1":
                    norm(1, m, m, x_s, xn, "tr1")
                elif name == "norm4":
                    norm(4, m, rest[0], x1, z, "trz")

        def take(eng, who, name, m):
            src = ring_of(name, m)
            on_act = who == "act"

            def copy(dst, src):
                return eng.activation(dst, src, ACT.Copy) if on_act else eng.tensor_copy(dst, src)

            made[name].wait(eng, m)
            if name in ("tr1", "trz"):
                if m >= 2:
                    made["k" if name == "tr1" else "h1"].wait(eng, m - 2)
                ins = copy((xT if name == "tr1" else zT)[:, m % 2, :], src[:, :])
            elif name in ("q", "k"):
                ins = copy(qk[:, m, 0 if name == "q" else 1, :], src[:, :])
            elif name == "hT":
                if m >= 2:
                    made["fc2"].wait(eng, m - 2)
                if on_act:
                    ins = eng.activation(h1T[:, m % 2, :], src[:, 0:P], ACT.Relu)
                else:
                    ins = eng.tensor_scalar(h1T[:, m % 2, :], src[:, 0:P], 0.0, None, ALU.max)
            else:
                c = int(name[1])
                if m == 0:
                    eng.wait_ge(s_w1, 32)
                if m >= 2:
                    made["y"].wait(eng, m - 2)
                dst = hid[:, m % 2, c, :]
                if on_act:
                    ins = eng.activation(dst, src[:, :], ACT.Relu, bias=b1_s[:, c:c + 1])
                else:
                    ins = eng.tensor_scalar(dst, src[:, :], b1_s[:, c:c + 1], 0.0, ALU.add, ALU.max)
            taken[name].done(ins, m)

        @block.scalar
        def _(eng):
            for name, m, *rest in ORDER:
                if name == "scores":
                    g, j, s = rest
                    i = seg_no[(m, g, j, s)]
                    width = min((g % per_batch) * GROUP + (j + 1) * P - s * SEGMENT, SEGMENT)
                    made["scores"].wait(eng, i)
                    s_exp.done(eng.activation(score[i % 2][:, 0:width], score[i % 2][:, 0:width], ACT.Exp, scale=SCALE,
                                              accum_out=rows[:, g, s, j:j + 1]), i)
                elif name in taken and own[name](m) == "act":
                    take(eng, "act", name, m)
                elif name in ("stat3", "stat5") and own[name](m) == "act":
                    k = int(name[4])
                    made["fc2" if k == 3 else "y"].wait(eng, m)
                    src = net_of("fc2" if k == 3 else "y", m)
                    for j in range(TILES):
                        last = eng.activation(junk[:, k // 4, j, :], src[:, j, :], ACT.Square, scale=SCALE,
                                              accum_out=mv[:, rest[0], slot[k], j, 1:2])
                    var[k].done(last, m)

        @block.vector
        def _(eng):
            own_chain = Chain(eng, s_dve)
            eng.memset(b2_f[:, :], 0.0).then_inc(s_zeroed, 1)
            eng.memset(fc2[:, :, :], 0.0).then_inc(s_zeroed, 1)

            def bn(k, m, g, src):
                for j in range(TILES):
                    last = eng.bn_stats(stats[:, g, slot[k], j, :], src(j))
                own_chain.link(last)
                for j in range(TILES):
                    last = eng.bn_aggr(mv[:, g, slot[k], j, :], stats[:, g, slot[k], j, :])
                if k in (1, 4):
                    own_chain.link(last)
                    last = eng.tensor_scalar(neg_mean[:, g, k // 4, :], mv[:, g, slot[k], :, 0], -1.0, None, ALU.mult)
                var[k].done(last, m)

            def setup_small():
                eng.memset(ones_b[:, :], 1.0)
                eng.memset(b2_s[:, :, :], 0.0)
                own_chain.link(eng.memset(h1e[:, :, :, :], 0.0))
                own_chain.link(eng.memset(h1e[:, :, :, INNER:INNER + 1], 1.0))
                eng.wait_ge(s_fc2, 16 * 2 * TILES)
                own_chain.link(eng.reduce_sum(means[:, 0:1], fc2[:, :, :], AX.XY))
                own_chain.link(eng.tensor_scalar(means[:, 1:2], means[:, 0:1], 1.0 / P, None, ALU.mult))
                for j in range(TILES):
                    r = slice(BLOCK * j, BLOCK * (j + 1))
                    last = eng.tensor_scalar(fc2[r, j, :], fc2[r, j, :], means[r, 1:2], None, ALU.subtract)
                last.then_inc(s_fc2c, 1)

            def setup_ffn():
                eng.wait_ge(s_w2, 16)
                own_chain.link(eng.reduce_sum(means[:, 2:4], w2_s[:, :, :], AX.X))
                own_chain.link(eng.tensor_scalar(means[:, 0:2], means[:, 2:4], 1.0 / P, None, ALU.mult))
                for c in range(HC):
                    last = eng.tensor_scalar(w2_s[:, c, :], w2_s[:, c, :], means[:, c:c + 1], None, ALU.subtract)
                own_chain.link(last)
                eng.wait_ge(s_b2, 48)
                own_chain.link(eng.reduce_sum(means[:, 2:3], b2_f[:, :], AX.X))
                own_chain.link(eng.tensor_scalar(means[:, 3:4], means[:, 2:3], 1.0 / P, None, ALU.mult))
                own_chain.link(eng.tensor_scalar(b2_f[:, :], b2_f[:, :], means[:, 3:4], None, ALU.subtract))
                own_chain.link(eng.tensor_copy(b2_h[:, 0, :], b2_f[:, :]))
                own_chain.link(eng.tensor_tensor(b2_r[:, 0, :], b2_f[:, :], b2_h[:, 0, :], ALU.subtract))
                own_chain.link(eng.tensor_copy(b2_h[:, 1, :], b2_r[:, 0, :]))
                own_chain.link(eng.tensor_tensor(b2_r[:, 1, :], b2_r[:, 0, :], b2_h[:, 1, :], ALU.subtract))
                own_chain.link(eng.tensor_copy(b2_h[:, 2, :], b2_r[:, 1, :]))
                for part in range(3):
                    r = slice(32 * part, 32 * part + 1)
                    last = eng.tensor_copy(b2_s[r, :, :], b2_h[r, part:part + 1, :].to_broadcast([1, TILES, P]))
                last.then_inc(s_b2c, 1)

            def rope(n):
                c = slice((n % per_batch) * GROUP, (n % per_batch + 1) * GROUP)
                cos, sin = (table[:, t, c].unsqueeze(1).to_broadcast([P, 2, GROUP]) for t in range(2))
                eng.wait_ge(s_table[n % per_batch], 16)
                taken["q"].wait(eng, n)
                taken["k"].wait(eng, n)
                eng.tensor_tensor(rot[:, n % 2, 0], qk[:, n], cos, ALU.mult)
                eng.wait_ge(s_swap[n], 32)
                own_chain.link(eng.tensor_tensor(rot[:, n % 2, 1], qk_swap[:, n], sin, ALU.mult))
                s_rope.done(eng.tensor_tensor(qk_r[:, n], rot[:, n % 2, 0], rot[:, n % 2, 1], ALU.add), n)

            def fc1_step(m, g):
                s_exp.wait(eng, last_seg[m])
                if m == 0:
                    eng.wait_ge(s_fc1, 32)
                o = rows[:, g, 0, :]
                if segments(g % per_batch) == 2:
                    own_chain.link(eng.tensor_tensor(osum[:, g, :], rows[:, g, 0, :], rows[:, g, 1, :], ALU.add))
                    o = osum[:, g, :]
                if m >= 2:
                    made["hT"].wait(eng, m - 2)
                h = h1e[:, m % 2, :, 0:INNER]
                wb, bb = (fc1[:, c, :].unsqueeze(1).to_broadcast([P, TILES, INNER]) for c in range(2))
                own_chain.link(eng.tensor_tensor(h, wb, o.unsqueeze(2).to_broadcast([P, TILES, INNER]), ALU.mult))
                s_fc1d.done(eng.tensor_tensor(h, h, bb, ALU.add), m)

            for name, m, *rest in ORDER:
                if name == "stat1":
                    eng.wait_ge(s_x[m], 16)
                    bn(1, m, m, lambda j: x_s[:, m, j, :])
                elif name == "rope":
                    rope(m)
                    if m == 0:
                        setup_small()
                    if m == 1:
                        setup_ffn()
                elif name == "fc1":
                    fc1_step(m, rest[0])
                elif name == "stat3" and own[name](m) == "dve":
                    made["fc2"].wait(eng, m)
                    bn(3, m, rest[0], lambda j: net_of("fc2", m)[:, j, :])
                elif name == "stat5" and own[name](m) == "dve":
                    made["y"].wait(eng, m)
                    bn(5, m, rest[0], lambda j: net_of("y", m)[:, j, :])
                elif name == "x1":
                    ready_r[3].wait(eng, m)
                    for j in range(TILES):
                        last = eng.scalar_tensor_tensor(x1[:, rest[0], j, :], net_of("fc2", m)[:, j, :],
                                                        rstd[:, rest[0], 1, j:j + 1], x_s[:, rest[0], j, :],
                                                        ALU.mult, ALU.add)
                    s_x1.done(last, m)
                elif name == "stat4":
                    s_x1.wait(eng, m)
                    bn(4, m, rest[0], lambda j: x1[:, rest[0], j, :])
                elif name == "out":
                    ready_r[5].wait(eng, m)
                    for j in range(TILES):
                        last = eng.scalar_tensor_tensor(out_s[:, rest[0], j, :], net_of("y", m)[:, j, :],
                                                        rstd[:, rest[0], 3, j:j + 1], x1[:, rest[0], j, :],
                                                        ALU.mult, ALU.add)
                    s_fin.done(last, m)
                elif name in taken and own[name](m) == "dve":
                    take(eng, "dve", name, m)

        @block.tensor
        def _(eng):
            eng.wait_ge(s_const, 1)

            def free_ring(name, m):
                k = ring_users.index((name, m))
                if k >= 2:
                    taken[ring_users[k - 2][0]].wait(eng, ring_users[k - 2][1])

            def free_net(name, m):
                k = net_users.index((name, m))
                if k >= 2:
                    who, n = net_users[k - 2]
                    (s_x1 if who == "fc2" else s_fin).wait(eng, n)

            for name, m, *rest in ORDER:
                if name in taken:
                    free_ring(name, m)
                    bank = ring_of(name, m)
                if name == "tr1" or name == "trz":
                    normed[1 if name == "tr1" else 4].wait(eng, m)
                    src = xn if name == "tr1" else z
                    for j in range(TILES):
                        mm = eng.transpose(bank[:, j * P:(j + 1) * P], src[:, m % 2, j, :], ident[:, :])
                    made[name].done(mm, m)
                elif name in ("q", "k"):
                    taken["tr1"].wait(eng, m)
                    if m == 0 and name == "q":
                        eng.wait_ge(s_wqk, 32)
                    made[name].done(eng.matmul(bank[:, :], wqk[:, 0 if name == "q" else 1, :], xT[:, m % 2, :],
                                               start=True, stop=True), m)
                elif name == "scores":
                    g, j, s = rest
                    i = seg_no[(m, g, j, s)]
                    gb, g0 = g % per_batch, g - g % per_batch
                    if i >= 2:
                        s_exp.wait(eng, i - 2)
                    if j == 0 and s == 0:
                        s_rope.wait(eng, g)
                    query = qk_r[:, g, 0, j * P:(j + 1) * P]
                    for c in range(s * PER_SEG, min(gb + 1, (s + 1) * PER_SEG)):
                        width = GROUP if c < gb else (j + 1) * P
                        at = (c - s * PER_SEG) * GROUP
                        mm = eng.matmul(score[i % 2][:, at:at + width], query, qk_r[:, g0 + c, 1, 0:width],
                                        start=True, stop=c < gb)
                    if c == gb:
                        mm = eng.matmul(score[i % 2][:, at + width - P:at + width], ident_b[:, :], later[:, :],
                                        start=False, stop=True)
                    made["scores"].done(mm, i)
                elif name == "hT":
                    s_fc1d.wait(eng, m)
                    made[name].done(eng.transpose(bank[:, 0:P], h1e[:, m % 2, :, :].rearrange("p j c -> p (j c)"),
                                                  ident[:, :]), m)
                elif name == "fc2":
                    taken["hT"].wait(eng, m)
                    if m == 0:
                        eng.wait_ge(s_fc2c, 1)
                    free_net(name, m)
                    made[name].done(eng.matmul(net_of(name, m)[:, :, :], h1T[:, m % 2, :], fc2[:, :, :],
                                               start=True, stop=True), m)
                elif name in ("h0", "h1"):
                    c = int(name[1])
                    taken["trz"].wait(eng, m)
                    if m == 0:
                        eng.wait_ge(s_w1, 32)
                    made[name].done(eng.matmul(bank[:, :], w1_s[:, c * P:(c + 1) * P], zT[:, m % 2, :],
                                               start=True, stop=True), m)
                elif name == "y":
                    taken["h0"].wait(eng, m)
                    taken["h1"].wait(eng, m)
                    if m == 0:
                        eng.wait_ge(s_b2c, 1)
                    free_net(name, m)
                    bank = net_of(name, m)
                    eng.matmul(bank[:, :, :], ones_b[:, :], b2_s[:, :, :], start=True, stop=False)
                    for j in range(TILES):
                        for c in range(HC):
                            mm = eng.matmul(bank[:, j, :], hid[:, m % 2, c, j * P:(j + 1) * P], w2_s[:, c, :],
                                            start=False, stop=(j == TILES - 1 and c == HC - 1))
                    made[name].done(mm, m)


def kernel(**inputs):
    import numpy as np
    import concourse.bacc as bacc
    from concourse.bass_utils import run_bass_kernel_spmd

    x = np.asarray(inputs["L0_attn_hidden_states"])
    _, length, dim = x.shape
    inv_freq = np.float32(32.0) ** (-np.arange(0, dim, 2, dtype=np.float32) / np.float32(dim))
    ang = np.arange(length, dtype=np.float32)[None, :] * inv_freq[:, None]
    cos, sin = np.cos(ang), np.sin(ang)
    tables = np.stack([np.concatenate([cos, cos]), np.concatenate([-sin, sin])], axis=1)
    arrays = {
        "x": x,
        "tables": tables.astype(np.dtype("bfloat16")),
        "wq_t": np.ascontiguousarray(np.asarray(inputs["L0_attn_Wq"]).T),
        "wk_t": np.ascontiguousarray(np.asarray(inputs["L0_attn_Wk"]).T),
        "fc1_w": np.asarray(inputs["L0_attn_fc1_w"]).reshape(-1),
        "fc1_b": np.asarray(inputs["L0_attn_fc1_b"]),
        "fc2_wt": np.ascontiguousarray(np.asarray(inputs["L0_attn_fc2_w"]).T),
        "fc2_b": np.asarray(inputs["L0_attn_fc2_b"]).reshape(1, -1),
        "w1": np.asarray(inputs["L0_ffn_W1"]),
        "b1": np.ascontiguousarray(np.asarray(inputs["L0_ffn_b1"]).reshape(-1, HC, P).transpose(0, 2, 1)),
        "w2": np.asarray(inputs["L0_ffn_W2"]),
        "b2": np.asarray(inputs["L0_ffn_b2"]),
    }
    nc = bacc.Bacc("TRN2", target_bir_lowering=False, num_devices=1)
    aps = {n: nc.dram_tensor(n, a.shape, mybir.dt.from_np(a.dtype), kind="ExternalInput").ap()
           for n, a in arrays.items()}
    out = nc.dram_tensor("out", x.shape, F32, kind="ExternalOutput").ap()
    build(nc, **aps, out=out)
    r = run_bass_kernel_spmd(nc, [arrays], core_ids=[0])
    return r.results[0]["out"]
```

```python
import concourse.bass as bass
from concourse import mybir
from contextlib import ExitStack

F32 = mybir.dt.float32
BF16 = mybir.dt.bfloat16
ALU = mybir.AluOpType
ACT = mybir.ActivationFunctionType
AX = mybir.AxisListType

P = 128
TILES = 4
GROUP = TILES * P
HALF = P // 2
INNER = 16
BLOCK = 32
HIDDEN = 256
HC = HIDDEN // P
EXPERT = 1
EPS = 1e-5
MASKED = -1e30
SEGMENT = 1024
PER_SEG = SEGMENT // GROUP


class Signal:

    def __init__(self, ctx, nc, name, owner):
        self.owner = owner
        self.sems = {}
        self.make = lambda who: ctx.enter_context(nc.semaphore(f"{name}_{who}"))

    def sem(self, who):
        if who not in self.sems:
            self.sems[who] = self.make(who)
        return self.sems[who]

    def done(self, instruction, n):
        instruction.then_inc(self.sem(self.owner(n)), 1)

    def wait(self, engine, n):
        who = self.owner(n)
        engine.wait_ge(self.sem(who), sum(self.owner(m) == who for m in range(n + 1)))


class Chain:

    def __init__(self, engine, sem):
        self.engine, self.sem, self.n = engine, sem, 0

    def link(self, instruction):
        self.n += 1
        instruction.then_inc(self.sem, 1)
        self.engine.wait_ge(self.sem, self.n)


def segments(gb):
    return -(-(gb + 1) // PER_SEG)


GROUP_ORDER = [0, 1, 4, 5, 2, 6, 3, 7]
FRONT_CUT = {0: [2, 2]}
BACK_CUT = {7: [2, 2]}

FRONT_START = [-0.0501, 1.3311, 2.8173, 6.977, 8.3002, 11.8574, 16.3204, 22.9598, 29.3254]
FRONT_STRETCH = [0.9674, 0.9919, 1.1235, 0.8768, 0.8728, 1.0482, 1.0206, 0.9695, 1.0]
FRONT_AT = {"stat1": 0.0, "rs1": 1.8998, "norm1": 2.6356, "norm1b": 2.745, "tr1": 5.2119, "+tr1": 5.2628,
            "q": 6.068, "+q": 6.4192, "k": 6.9826, "+k": 7.4968, "swap": 10.303, "cos": 9.1731, "rope": 12.0307}
MIDDLE_START = [10.4177, 15.213, 20.1807, 25.6794, 30.6768, 36.7086, 42.8594, 49.3608, 52.9793]
MIDDLE_LASTS = [2.2872, 3.2904, 2.0, 4.4351, 5.908, 4.2631, 5.7392, 3.5926, 5.4644]
EXP_LAG = 0.3861
BACK_START = [15.003, 20.4605, 25.2532, 31.8693, 36.9232, 41.5804, 49.2414, 53.58, 57.7583]
BACK_STRETCH = [1.0086, 0.994, 1.0328, 0.9648, 0.9918, 1.0083, 0.9815, 1.0997, 0.9882]
BACK_AFTER = {"sum": 0.0585, "hT": 1.8025, "+hT": 1.8228, "fc2": 2.8994, "stat3": 3.1456, "rs3": 4.5266,
              "x1": 5.4964, "stat4": 6.1013, "rs4": 6.9293, "norm4": 8.2568, "norm4b": 8.3669, "trz": 10.5165,
              "+trz": 10.8025, "h0": 12.5937, "+h0": 12.8176, "h1": 13.8046, "+h1": 14.0617, "y": 16.868,
              "stat5": 17.5337, "rs5": 18.6609, "out": 20.8786}

DOES = {"cos": "PDPPPPDDD", "tr1": "DAAAAAAAD", "q": "ADAAAAAAD", "k": "AAAAAAAAA", "hT": "AAAAAAAAA",
        "stat3": "AAAAADAAA", "trz": "AAAADDDDD", "h0": "AADDDAADA", "h1": "AAAADAAAA", "stat5": "DDDAAAAAA",
        "norm1": "DDPDPPPDD", "norm1b": "PPPPPPDDD", "norm4": "PPDPPPPDD", "norm4b": "DDPPDDPDD"}


def cut(groups, cuts):
    units = []
    for g in groups:
        j = 0
        for n in cuts.get(g, [TILES]):
            units.append((g, j, n))
            j += n
    return units


def plan(per_batch):
    fronts = cut(GROUP_ORDER, FRONT_CUT)
    backs = cut(GROUP_ORDER, BACK_CUT)
    steps = []

    def at(t, name, *args):
        steps.append((t, len(steps), (name, *args)))

    for n, t in enumerate(FRONT_START):
        for name, after in FRONT_AT.items():
            at(t + after * FRONT_STRETCH[n], name, n)
    for m, (g, j0, tiles) in enumerate(backs):
        parts = [(j, s) for j in range(j0, j0 + tiles) for s in range(segments(g % per_batch))]
        for i, (j, s) in enumerate(parts):
            t = MIDDLE_START[m] + MIDDLE_LASTS[m] * i / len(parts)
            at(t, "scores", m, g, j, s)
            at(t + EXP_LAG, "exp", m, g, j, s)
        for name, after in BACK_AFTER.items():
            at(BACK_START[m] + after * BACK_STRETCH[m], name, m)
    order = [step for _, _, step in sorted(steps)]
    for name in {step[0] for step in order}:
        assert [s for s in order if s[0] == name] == [s for _, _, s in steps if s[0] == name], name
    return fronts, backs, order


def build(nc, x, tables, wqk_t, fc1_wb, fc2_wb, w1, b1, w2, b2, out):
    batch, length, dim = x.shape
    n_groups = batch * length // GROUP
    per_batch = length // GROUP
    fronts, backs, ORDER = plan(per_batch)
    engine_of = {"A": "act", "D": "dve", "P": "pool"}
    own = {name: (lambda n, who=who: engine_of[who[n]]) for name, who in DOES.items()}
    SCALE = 1.0 / float(dim) ** 0.5

    x_v = x.rearrange("b (g j p) d -> (b g) p j d", j=TILES, p=P)
    out_v = out.rearrange("b (g j p) d -> (b g) p j d", j=TILES, p=P)

    with ExitStack() as ctx:
        def sb(name, shape, dt):
            return ctx.enter_context(nc.sbuf_tensor(name, shape, dt))

        def sem(name):
            return ctx.enter_context(nc.semaphore(name))

        def signal(name, owner):
            return Signal(ctx, nc, name, owner if callable(owner) else lambda n: owner)

        ident = sb("ident", [P, P], F32)
        ident_b = sb("ident_b", [P, P], BF16)
        later = sb("later", [P, P], BF16)
        ones_b = sb("ones_b", [P, P], BF16)
        half_neg = sb("half_neg", [P, TILES], F32)
        table = sb("table", [P, 2, length], BF16)
        wqk = sb("wqk", [P, 2, P], F32)
        fc1 = sb("fc1", [P, 2], F32)
        fc2 = sb("fc2", [P, TILES, P], F32)
        w1_s = sb("w1_s", [P, HIDDEN], F32)
        b1_s = sb("b1_s", [P, HC], F32)
        w2_s = sb("w2_s", [P, HC, P], F32)
        b2_f = sb("b2_f", [P, P], F32)
        b2_r = sb("b2_r", [P, 2, P], F32)
        b2_h = sb("b2_h", [P, 3, P], BF16)
        b2_s = sb("b2_s", [P, TILES, P], BF16)
        means = sb("means", [P, 4], F32)
        x_s = sb("x_s", [P, n_groups, TILES, P], F32)
        xn = sb("xn", [P, 2, TILES, P], F32)
        xT = sb("xT", [P, 2, GROUP], F32)
        qk = sb("qk", [P, n_groups, 2, GROUP], BF16)
        qk_swap = sb("qk_swap", [P, n_groups, 2, GROUP], BF16)
        rot = sb("rot", [P, 2, 2, 2, GROUP], BF16)
        qk_r = sb("qk_r", [P, n_groups, 2, GROUP], BF16)
        rows = sb("rows", [P, n_groups, 2, TILES], F32)
        osum = sb("osum", [P, 2, TILES, BLOCK], F32)
        h1T = sb("h1T", [P, 2, P], F32)
        x1 = sb("x1", [P, n_groups, TILES, P], F32)
        z = sb("z", [P, 2, TILES, P], F32)
        zT = sb("zT", [P, 2, GROUP], F32)
        hid = sb("hid", [P, 2, HC, GROUP], F32)
        out_s = sb("out_s", [P, n_groups, TILES, P], F32)
        junk = sb("junk", [P, len(backs), 2, TILES, P], BF16)
        stats = sb("stats", [P, n_groups, 4, TILES, 6], F32)
        mv = sb("mv", [P, n_groups, 4, TILES, 2], F32)
        neg_mean = sb("neg_mean", [P, n_groups, TILES], F32)
        ve = sb("ve", [P, n_groups, 4, TILES], F32)
        rstd = sb("rstd", [P, n_groups, 4, TILES], F32)
        score = [ctx.enter_context(nc.psum_tensor(f"score{i}", [P, SEGMENT], F32)) for i in range(2)]
        ring = [ctx.enter_context(nc.psum_tensor(f"ring{i}", [P, GROUP], F32)) for i in range(2)]
        net = [ctx.enter_context(nc.psum_tensor(f"net{i}", [P, TILES, P], F32)) for i in range(2)]

        s_x = [sem(f"s_x{n}") for n in range(len(fronts))]
        s_table = [sem(f"s_table{c}") for c in range(per_batch)]
        s_swap = [sem(f"s_swap{n}") for n in range(len(fronts))]
        s_wqk, s_fc1, s_fc2, s_w1, s_w2, s_b2 = (sem("s_" + n) for n in ["wqk", "fc1", "fc2", "w1", "w2", "b2"])
        s_out = sem("s_out")
        s_zeroed, s_const, s_fc2c, s_b2c = (sem("s_" + n) for n in ["zeroed", "const", "fc2c", "b2c"])
        s_dve, s_pool = sem("s_dve"), sem("s_pool")

        made = {n: signal("made_" + n, "pe") for n in ["tr1", "q", "k", "scores", "hT", "fc2", "trz", "h0", "h1", "y"]}
        taken = {n: signal("taken_" + n, own[n]) for n in ["tr1", "q", "k", "hT", "trz", "h0", "h1"]}
        takes = {"+" + n: n for n in taken}
        var = {1: signal("var1", "dve"), 3: signal("var3", own["stat3"]),
               4: signal("var4", "dve"), 5: signal("var5", own["stat5"])}
        ready_r = {n: signal(f"rstd{n}", "pool") for n in [1, 3, 4, 5]}
        normed = {n: signal(n + "_done", own[n]) for n in ["norm1", "norm1b", "norm4", "norm4b"]}
        s_cos = signal("cos", own["cos"])
        s_rope = signal("roped", "dve")
        s_exp = signal("exps", "act")
        s_sums = signal("sums", "dve")
        s_x1 = signal("x1d", "dve")
        s_fin = signal("fin", "dve")

        slot = {1: 0, 3: 1, 4: 2, 5: 3}

        ring_users = [(st[0], st[1]) for st in ORDER if st[0] in taken]
        net_users = [(st[0], st[1]) for st in ORDER if st[0] in ("fc2", "y")]
        segs = [st[1:] for st in ORDER if st[0] == "scores"]
        seg_no = {st: i for i, st in enumerate(segs)}
        last_seg = [max(i for i, st in enumerate(segs) if st[0] == m) for m in range(len(backs))]
        front_of = {(g, j): n for n, (g, j0, tiles) in enumerate(fronts) for j in range(j0, j0 + tiles)}

        def ring_of(name, n):
            return ring[ring_users.index((name, n)) % 2]

        def net_of(name, n):
            return net[net_users.index((name, n)) % 2]

        block = ctx.enter_context(nc.Block())

        def load_x(eng, n):
            g, j0, tiles = fronts[n]
            eng.dma_start(x_s[:, g, j0:j0 + tiles], x_v[g][:, j0:j0 + tiles]).then_inc(s_x[n], 16)

        def load_table(eng, c):
            eng.dma_start(table[:, :, c * GROUP:(c + 1) * GROUP],
                          tables[:, :, c * GROUP:(c + 1) * GROUP]).then_inc(s_table[c], 16)

        @block.sync
        def _(eng):
            load_x(eng, 0)
            load_x(eng, 1)
            eng.dma_start(wqk[:, :, :], wqk_t).then_inc(s_wqk, 16)
            load_x(eng, 2)
            load_table(eng, 0)
            load_x(eng, 3)
            load_table(eng, 1)
            load_x(eng, 4)
            eng.wait_ge(s_zeroed, 2)
            for j in range(TILES):
                eng.dma_start(fc2[BLOCK * j:BLOCK * j + INNER + 1, j, :], fc2_wb).then_inc(s_fc2, 16)
                eng.dma_start(fc1[BLOCK * j:BLOCK * j + INNER + 1, :], fc1_wb).then_inc(s_fc1, 16)
            eng.dma_start(w1_s[:, :], w1[EXPERT]).then_inc(s_w1, 16)
            eng.dma_start(b1_s[:, :], b1[EXPERT]).then_inc(s_w1, 16)
            eng.dma_start(w2_s[:, :, :], w2[EXPERT].rearrange("(c p) o -> p c o", p=P)).then_inc(s_w2, 16)
            for part in range(3):
                eng.dma_start(b2_f[32 * part:32 * part + 1, :], b2[EXPERT:EXPERT + 1, :]).then_inc(s_b2, 16)
            late = [lambda: load_x(eng, 5), lambda: load_table(eng, 2), lambda: load_x(eng, 6),
                    lambda: load_table(eng, 3), *[lambda n=n: load_x(eng, n) for n in range(7, len(fronts))]]
            for name, n, *rest in ORDER:
                if name == "swap":
                    g, j0, tiles = fronts[n]
                    c = slice(j0 * P, (j0 + tiles) * P)
                    taken["q"].wait(eng, n)
                    taken["k"].wait(eng, n)
                    eng.dma_start(qk_swap[0:HALF, g, :, c], qk[HALF:P, g, :, c]).then_inc(s_swap[n], 16)
                    eng.dma_start(qk_swap[HALF:P, g, :, c], qk[0:HALF, g, :, c]).then_inc(s_swap[n], 16)
                    for load in late[3 * n:3 * n + 3]:
                        load()
                if name == "out":
                    g, j0, tiles = backs[n]
                    s_fin.wait(eng, n)
                    eng.dma_start(out_v[g][:, j0:j0 + tiles], out_s[:, g, j0:j0 + tiles]).then_inc(s_out, 16)
            eng.wait_ge(s_out, 16 * len(backs))

        def rope_part(n):
            g, j0, tiles = fronts[n]
            return g, slice(j0 * P, (j0 + tiles) * P), tiles * P, (g % per_batch) * GROUP + j0 * P

        def cos_product(eng, n):
            g, c, w, t0 = rope_part(n)
            eng.wait_ge(s_table[g % per_batch], 16)
            taken["q"].wait(eng, n)
            taken["k"].wait(eng, n)
            if n >= 2:
                s_rope.wait(eng, n - 2)
            if own["cos"](n) == "pool":
                for t in range(2):
                    last = eng.tensor_tensor(rot[:, n % 2, 0, t, 0:w], qk[:, g, t, c], table[:, 0, t0:t0 + w],
                                             ALU.mult)
            else:
                cos = table[:, 0, t0:t0 + w].unsqueeze(1).to_broadcast([P, 2, w])
                last = eng.tensor_tensor(rot[:, n % 2, 0, :, 0:w], qk[:, g, :, c], cos, ALU.mult)
            s_cos.done(last, n)

        def norm(eng, name, m):
            k = int(name[4])
            g, j0, tiles = fronts[m] if k == 1 else backs[m]
            src, dst, reader = (x_s, xn, "tr1") if k == 1 else (x1, z, "trz")
            if m >= 2:
                made[reader].wait(eng, m - 2)
            ready_r[k].wait(eng, m)
            for j in range(tiles // 2, tiles) if name[-1] == "b" else range(tiles // 2):
                last = eng.tensor_scalar(dst[:, m % 2, j, :], src[:, g, j0 + j, :],
                                         neg_mean[:, g, j0 + j:j0 + j + 1],
                                         rstd[:, g, slot[k], j0 + j:j0 + j + 1], ALU.add, ALU.mult)
            normed[name].done(last, m)

        @block.gpsimd
        def _(eng):
            own_chain = Chain(eng, s_pool)
            eng.memset(half_neg[:, :], -0.5)
            eng.memset(ident[:, :], 0.0)
            eng.memset(ident_b[:, :], 0.0)
            own_chain.link(eng.memset(later[:, :], 0.0))
            eng.affine_select(out=ident[:, :], in_=ident[:, :], compare_op=ALU.not_equal, fill=1.0, base=0,
                              pattern=[[-1, P]], channel_multiplier=1)
            eng.affine_select(out=ident_b[:, :], in_=ident_b[:, :], compare_op=ALU.not_equal, fill=1.0, base=0,
                              pattern=[[-1, P]], channel_multiplier=1)
            eng.affine_select(out=later[:, :], in_=later[:, :], compare_op=ALU.is_ge, fill=MASKED, base=0,
                              pattern=[[-1, P]], channel_multiplier=1).then_inc(s_const, 1)

            for name, m, *rest in ORDER:
                if name in ("rs1", "rs3", "rs4", "rs5"):
                    k = int(name[2])
                    g, j0, tiles = fronts[m] if k == 1 else backs[m]
                    t = slice(j0, j0 + tiles)
                    var[k].wait(eng, m)
                    own_chain.link(eng.tensor_scalar(ve[:, g, slot[k], t], mv[:, g, slot[k], t, 1], EPS, None, ALU.add))
                    ready_r[k].done(eng.tensor_tensor(rstd[:, g, slot[k], t], ve[:, g, slot[k], t],
                                                      half_neg[:, 0:tiles], ALU.pow), m)
                elif name in normed and own[name](m) == "pool":
                    norm(eng, name, m)
                elif name == "cos" and own["cos"](m) == "pool":
                    cos_product(eng, m)

        def take(eng, who, name, m):
            src = ring_of(name, m)
            on_act = who == "act"
            g, j0, tiles = fronts[m] if name in ("tr1", "q", "k") else backs[m]
            w = tiles * P

            def copy(dst, src):
                return eng.activation(dst, src, ACT.Copy) if on_act else eng.tensor_copy(dst, src)

            made[name].wait(eng, m)
            if name in ("tr1", "trz"):
                if m >= 2:
                    made["k" if name == "tr1" else "h1"].wait(eng, m - 2)
                ins = copy((xT if name == "tr1" else zT)[:, m % 2, 0:w], src[:, 0:w])
            elif name in ("q", "k"):
                ins = copy(qk[:, g, 0 if name == "q" else 1, j0 * P:j0 * P + w], src[:, 0:w])
            elif name == "hT":
                if m >= 2:
                    made["fc2"].wait(eng, m - 2)
                if m == 0:
                    eng.wait_ge(s_fc1, 16 * TILES)
                r = tiles * BLOCK
                ins = eng.activation(h1T[0:r, m % 2, :], src[0:r, 0:P], ACT.Relu, scale=fc1[0:r, 0:1],
                                     bias=fc1[0:r, 1:2])
            else:
                c = int(name[1])
                if m == 0:
                    eng.wait_ge(s_w1, 32)
                if m >= 2:
                    made["y"].wait(eng, m - 2)
                dst = hid[:, m % 2, c, 0:w]
                if on_act:
                    ins = eng.activation(dst, src[:, 0:w], ACT.Relu, bias=b1_s[:, c:c + 1])
                else:
                    ins = eng.tensor_scalar(dst, src[:, 0:w], b1_s[:, c:c + 1], 0.0, ALU.add, ALU.max)
            taken[name].done(ins, m)

        @block.scalar
        def _(eng):
            for name, m, *rest in ORDER:
                if name == "exp":
                    g, j, s = rest
                    i = seg_no[(m, g, j, s)]
                    width = min((g % per_batch) * GROUP + (j + 1) * P - s * SEGMENT, SEGMENT)
                    made["scores"].wait(eng, i)
                    s_exp.done(eng.activation(score[i % 2][:, 0:width], score[i % 2][:, 0:width], ACT.Exp, scale=SCALE,
                                              accum_out=rows[:, g, s, j:j + 1]), i)
                elif name in takes and own[takes[name]](m) == "act":
                    take(eng, "act", takes[name], m)
                elif name in ("stat3", "stat5") and own[name](m) == "act":
                    k = int(name[4])
                    made["fc2" if k == 3 else "y"].wait(eng, m)
                    src = net_of("fc2" if k == 3 else "y", m)
                    g, j0, tiles = backs[m]
                    for j in range(tiles):
                        last = eng.activation(junk[:, m, k // 4, j, :], src[:, j, :], ACT.Square, scale=SCALE,
                                              accum_out=mv[:, g, slot[k], j0 + j, 1:2])
                    var[k].done(last, m)

        @block.vector
        def _(eng):
            own_chain = Chain(eng, s_dve)
            eng.memset(b2_f[:, :], 0.0).then_inc(s_zeroed, 1)
            eng.memset(fc1[:, :], 0.0)
            eng.memset(fc2[:, :, :], 0.0).then_inc(s_zeroed, 1)

            def bn(k, m, src):
                g, j0, tiles = fronts[m] if k == 1 else backs[m]
                for j in range(tiles):
                    last = eng.bn_stats(stats[:, g, slot[k], j0 + j, :], src(j))
                own_chain.link(last)
                for j in range(j0, j0 + tiles):
                    last = eng.bn_aggr(mv[:, g, slot[k], j, :], stats[:, g, slot[k], j, :])
                if k == 1:
                    own_chain.link(last)
                    last = eng.tensor_scalar(neg_mean[:, g, j0:j0 + tiles],
                                             mv[:, g, slot[k], j0:j0 + tiles, 0], -1.0, None, ALU.mult)
                var[k].done(last, m)

            def setup_small():
                eng.memset(ones_b[:, :], 1.0)
                eng.memset(b2_s[:, :, :], 0.0)
                eng.wait_ge(s_fc2, 16 * TILES)
                own_chain.link(eng.reduce_sum(means[:, 0:1], fc2[:, :, :], AX.XY))
                own_chain.link(eng.tensor_scalar(means[:, 1:2], means[:, 0:1], 1.0 / P, None, ALU.mult))
                for j in range(TILES):
                    r = slice(BLOCK * j, BLOCK * (j + 1))
                    last = eng.tensor_scalar(fc2[r, j, :], fc2[r, j, :], means[r, 1:2], None, ALU.subtract)
                last.then_inc(s_fc2c, 1)

            def setup_ffn():
                eng.wait_ge(s_w2, 16)
                own_chain.link(eng.reduce_sum(means[:, 2:4], w2_s[:, :, :], AX.X))
                own_chain.link(eng.tensor_scalar(means[:, 0:2], means[:, 2:4], 1.0 / P, None, ALU.mult))
                for c in range(HC):
                    last = eng.tensor_scalar(w2_s[:, c, :], w2_s[:, c, :], means[:, c:c + 1], None, ALU.subtract)
                own_chain.link(last)
                eng.wait_ge(s_b2, 48)
                own_chain.link(eng.reduce_sum(means[:, 2:3], b2_f[:, :], AX.X))
                own_chain.link(eng.tensor_scalar(means[:, 3:4], means[:, 2:3], 1.0 / P, None, ALU.mult))
                own_chain.link(eng.tensor_scalar(b2_f[:, :], b2_f[:, :], means[:, 3:4], None, ALU.subtract))
                own_chain.link(eng.tensor_copy(b2_h[:, 0, :], b2_f[:, :]))
                own_chain.link(eng.tensor_tensor(b2_r[:, 0, :], b2_f[:, :], b2_h[:, 0, :], ALU.subtract))
                own_chain.link(eng.tensor_copy(b2_h[:, 1, :], b2_r[:, 0, :]))
                own_chain.link(eng.tensor_tensor(b2_r[:, 1, :], b2_r[:, 0, :], b2_h[:, 1, :], ALU.subtract))
                own_chain.link(eng.tensor_copy(b2_h[:, 2, :], b2_r[:, 1, :]))
                for part in range(3):
                    r = slice(32 * part, 32 * part + 1)
                    last = eng.tensor_copy(b2_s[r, :, :], b2_h[r, part:part + 1, :].to_broadcast([1, TILES, P]))
                last.then_inc(s_b2c, 1)

            def rope(n):
                g, c, w, t0 = rope_part(n)
                s_cos.wait(eng, n)
                eng.wait_ge(s_swap[n], 32)
                sin = table[:, 1, t0:t0 + w].unsqueeze(1).to_broadcast([P, 2, w])
                own_chain.link(eng.tensor_tensor(rot[:, n % 2, 1, :, 0:w], qk_swap[:, g, :, c], sin, ALU.mult))
                s_rope.done(eng.tensor_tensor(qk_r[:, g, :, c], rot[:, n % 2, 0, :, 0:w], rot[:, n % 2, 1, :, 0:w],
                                              ALU.add), n)

            def row_sums(m):
                g, j0, tiles = backs[m]
                s_exp.wait(eng, last_seg[m])
                if m >= 2:
                    made["hT"].wait(eng, m - 2)
                dst = osum[:, m % 2, 0:tiles, :]
                parts = [rows[:, g, s, j0:j0 + tiles].unsqueeze(2).to_broadcast([P, tiles, BLOCK]) for s in range(2)]
                if segments(g % per_batch) == 2:
                    s_sums.done(eng.tensor_tensor(dst, parts[0], parts[1], ALU.add), m)
                else:
                    s_sums.done(eng.tensor_copy(dst, parts[0]), m)

            def add_net(k, m, dst, prev):
                g, j0, tiles = backs[m]
                bank = net_of("fc2" if k == 3 else "y", m)
                ready_r[k].wait(eng, m)
                for j in range(tiles):
                    last = eng.scalar_tensor_tensor(dst[:, g, j0 + j, :], bank[:, j, :],
                                                    rstd[:, g, slot[k], j0 + j:j0 + j + 1], prev[:, g, j0 + j, :],
                                                    ALU.mult, ALU.add)
                return last

            for name, m, *rest in ORDER:
                if name == "stat1":
                    g, j0, _ = fronts[m]
                    eng.wait_ge(s_x[m], 16)
                    bn(1, m, lambda j: x_s[:, g, j0 + j, :])
                elif name == "rope":
                    rope(m)
                    if m == 1:
                        setup_small()
                    if m == 2:
                        setup_ffn()
                elif name == "sum":
                    row_sums(m)
                elif name in ("stat3", "stat5") and own[name](m) == "dve":
                    net_name = "fc2" if name == "stat3" else "y"
                    made[net_name].wait(eng, m)
                    bn(int(name[4]), m, lambda j: net_of(net_name, m)[:, j, :])
                elif name == "x1":
                    s_x1.done(add_net(3, m, x1, x_s), m)
                elif name == "stat4":
                    g, j0, _ = backs[m]
                    s_x1.wait(eng, m)
                    bn(4, m, lambda j: x1[:, g, j0 + j, :])
                elif name == "out":
                    s_fin.done(add_net(5, m, out_s, x1), m)
                elif name in normed and own[name](m) == "dve":
                    norm(eng, name, m)
                elif name == "cos" and own["cos"](m) == "dve":
                    cos_product(eng, m)
                elif name in takes and own[takes[name]](m) == "dve":
                    take(eng, "dve", takes[name], m)

        @block.tensor
        def _(eng):
            eng.wait_ge(s_const, 1)

            def free_ring(name, m):
                k = ring_users.index((name, m))
                if k >= 2:
                    taken[ring_users[k - 2][0]].wait(eng, ring_users[k - 2][1])

            def free_net(name, m):
                k = net_users.index((name, m))
                if k >= 2:
                    who, n = net_users[k - 2]
                    (s_x1 if who == "fc2" else s_fin).wait(eng, n)

            for name, m, *rest in ORDER:
                if name in taken:
                    free_ring(name, m)
                    bank = ring_of(name, m)
                if name != "scores":
                    g, j0, tiles = (fronts if name in FRONT_AT else backs)[m]
                    w = tiles * P
                if name == "tr1" or name == "trz":
                    for half in ("norm1", "norm1b") if name == "tr1" else ("norm4", "norm4b"):
                        normed[half].wait(eng, m)
                    src = xn if name == "tr1" else z
                    for j in range(tiles):
                        mm = eng.transpose(bank[:, j * P:(j + 1) * P], src[:, m % 2, j, :], ident[:, :])
                    made[name].done(mm, m)
                elif name in ("q", "k"):
                    taken["tr1"].wait(eng, m)
                    if m == 0 and name == "q":
                        eng.wait_ge(s_wqk, 16)
                    made[name].done(eng.matmul(bank[:, 0:w], wqk[:, 0 if name == "q" else 1, :], xT[:, m % 2, 0:w],
                                               start=True, stop=True), m)
                elif name == "scores":
                    g, j, s = rest
                    i = seg_no[(m, g, j, s)]
                    gb, g0 = g % per_batch, g - g % per_batch
                    if i >= 2:
                        s_exp.wait(eng, i - 2)
                    if s == 0:
                        s_rope.wait(eng, front_of[g, j])
                    query = qk_r[:, g, 0, j * P:(j + 1) * P]
                    for c in range(s * PER_SEG, min(gb + 1, (s + 1) * PER_SEG)):
                        width = GROUP if c < gb else (j + 1) * P
                        at = (c - s * PER_SEG) * GROUP
                        mm = eng.matmul(score[i % 2][:, at:at + width], query, qk_r[:, g0 + c, 1, 0:width],
                                        start=True, stop=c < gb)
                    if c == gb:
                        mm = eng.matmul(score[i % 2][:, at + width - P:at + width], ident_b[:, :], later[:, :],
                                        start=False, stop=True)
                    made["scores"].done(mm, i)
                elif name == "hT":
                    s_sums.wait(eng, m)
                    o = osum[:, m % 2, 0:tiles, :].rearrange("p j c -> p (j c)")
                    made[name].done(eng.transpose(bank[0:tiles * BLOCK, 0:P], o, ident[:, :]), m)
                elif name == "fc2":
                    taken["hT"].wait(eng, m)
                    if m == 0:
                        eng.wait_ge(s_fc2c, 1)
                    free_net(name, m)
                    made[name].done(eng.matmul(net_of(name, m)[:, 0:tiles, :], h1T[0:tiles * BLOCK, m % 2, :],
                                               fc2[0:tiles * BLOCK, 0:tiles, :],
                                               start=True, stop=True), m)
                elif name in ("h0", "h1"):
                    c = int(name[1])
                    taken["trz"].wait(eng, m)
                    if m == 0:
                        eng.wait_ge(s_w1, 32)
                    made[name].done(eng.matmul(bank[:, 0:w], w1_s[:, c * P:(c + 1) * P], zT[:, m % 2, 0:w],
                                               start=True, stop=True), m)
                elif name == "y":
                    taken["h0"].wait(eng, m)
                    taken["h1"].wait(eng, m)
                    if m == 0:
                        eng.wait_ge(s_b2c, 1)
                    free_net(name, m)
                    bank = net_of(name, m)
                    eng.matmul(bank[:, 0:tiles, :], ones_b[:, :], b2_s[:, 0:tiles, :], start=True, stop=False)
                    for j in range(tiles):
                        for c in range(HC):
                            mm = eng.matmul(bank[:, j, :], hid[:, m % 2, c, j * P:(j + 1) * P], w2_s[:, c, :],
                                            start=False, stop=(j == tiles - 1 and c == HC - 1))
                    made[name].done(mm, m)


def kernel(**inputs):
    import numpy as np
    import concourse.bacc as bacc
    from concourse.bass_utils import run_bass_kernel_spmd

    x = np.asarray(inputs["L0_attn_hidden_states"])
    _, length, dim = x.shape
    inv_freq = np.float32(32.0) ** (-np.arange(0, dim, 2, dtype=np.float32) / np.float32(dim))
    ang = np.arange(length, dtype=np.float32)[None, :] * inv_freq[:, None]
    cos, sin = np.cos(ang), np.sin(ang)
    tables = np.stack([np.concatenate([cos, cos]), np.concatenate([-sin, sin])], axis=1)
    arrays = {
        "x": x,
        "tables": tables.astype(np.dtype("bfloat16")),
        "wqk_t": np.stack([np.asarray(inputs["L0_attn_Wq"]).T, np.asarray(inputs["L0_attn_Wk"]).T], axis=1),
        "fc1_wb": np.concatenate([np.stack([np.asarray(inputs["L0_attn_fc1_w"]).reshape(-1),
                                            np.asarray(inputs["L0_attn_fc1_b"])], axis=1),
                                  np.array([[0.0, 1.0]], np.float32)]),
        "fc2_wb": np.concatenate([np.asarray(inputs["L0_attn_fc2_w"]).T,
                                  np.asarray(inputs["L0_attn_fc2_b"]).reshape(1, -1)]),
        "w1": np.asarray(inputs["L0_ffn_W1"]),
        "b1": np.ascontiguousarray(np.asarray(inputs["L0_ffn_b1"]).reshape(-1, HC, P).transpose(0, 2, 1)),
        "w2": np.asarray(inputs["L0_ffn_W2"]),
        "b2": np.asarray(inputs["L0_ffn_b2"]),
    }
    nc = bacc.Bacc("TRN2", target_bir_lowering=False, num_devices=1)
    aps = {n: nc.dram_tensor(n, a.shape, mybir.dt.from_np(a.dtype), kind="ExternalInput").ap()
           for n, a in arrays.items()}
    out = nc.dram_tensor("out", x.shape, F32, kind="ExternalOutput").ap()
    build(nc, **aps, out=out)
    r = run_bass_kernel_spmd(nc, [arrays], core_ids=[0])
    return r.results[0]["out"]
```
